# Optimizing a Trainium2 kernel written in Bass

```python
import numpy as np
import jax
import jax.numpy as jnp

def _softmax(x, axis=-1):
    return jax.nn.softmax(x, axis=axis)

def _gelu(x):
    return jax.nn.gelu(x, approximate=True)

def _silu(x):
    return jax.nn.silu(x)

def _sigmoid(x):
    return jax.nn.sigmoid(x)

def _layernorm(x, axis=-1, eps=1e-05):
    m = jnp.mean(x, axis=axis, keepdims=True)
    v = jnp.var(x, axis=axis, keepdims=True)
    return (x - m) / jnp.sqrt(v + eps)

def _scatter_add(tgt, idx, src, axis=0):
    return tgt.at[idx].add(src)

def _segment_sum(src, seg, n):
    return jax.ops.segment_sum(src, seg, n)
kernel_name = 'mk_rec_standalone_d1_rec_r8_12985b'

def setup_inputs(seed: int=0):
    np.random.seed(seed)
    _w = jnp.asarray

    def _rec_inputs():
        import jax
        import jax.numpy as jnp
        _rk = jax.random.key(seed)
        r_ids = jax.random.randint(jax.random.fold_in(_rk, 1), (512, 32, 20), 0, 12500, jnp.int32)
        r_lengths = jax.random.randint(jax.random.fold_in(_rk, 2), (512, 32), 0, 21, jnp.int32)
        return (r_ids, r_lengths)
    r_ids, r_lengths = _rec_inputs()

    def _L0_rec_setup():
        import jax, jax.numpy as jnp
        import numpy as np
        B, F, V, L, E = (512, 32, 12500, 20, 64)
        key = jax.random.key(seed)
        k1, k2, k3 = jax.random.split(key, 3)
        ids = jax.random.randint(k1, (B, F, L), 0, V, dtype=jnp.int64)
        lengths = jax.random.randint(k2, (B, F), 0, L + 1, dtype=jnp.int64)
        tables = jax.random.normal(k3, (F, V, E), dtype=jnp.float32) * 0.02
        return {'ids': ids, 'lengths': lengths, 'tables': tables}
    _L0_rec_all = _L0_rec_setup()
    _L0_rec_in = {k: v for k, v in _L0_rec_all.items() if k in ('tables',)}
    del _L0_rec_all
    return {'r_ids': r_ids, 'r_lengths': r_lengths, 'L0_rec_tables': _L0_rec_in['tables']}

def reference(r_ids, r_lengths, L0_rec_tables):
    import jax
    import jax.numpy as jnp

    def _L0_rec_ref(ids, lengths, tables):
        import jax, jax.numpy as jnp
        import numpy as np
        B, F, V, L, E = (512, 32, 12500, 20, 64)
        F_, V_, E_ = tables.shape
        Bq, _, L_ = ids.shape
        flat = tables.reshape(F_ * V_, E_)
        offs = jnp.arange(F_, dtype=ids.dtype)[None, :, None] * V_
        emb = flat[ids + offs]
        mask = (jnp.arange(L_) < lengths[..., None]).astype(emb.dtype)
        pooled = jnp.einsum('bfle,bfl->bfe', emb, mask)
        out = pooled.reshape(Bq, F_ * E_)
        return jnp.nan_to_num(out)
    y = _L0_rec_ref(r_ids, r_lengths, L0_rec_tables)
    return y

_drawn_inputs = setup_inputs


def setup_inputs(seed=0):
    import zlib

    import numpy as np

    out = dict(_drawn_inputs(seed))
    spreads = {}
    factors = {}
    for name, (base, spread) in spreads.items():
        noise = np.random.default_rng([zlib.crc32(name.encode()), seed]).standard_normal(out[name].shape)
        drawn = base * np.exp(spread * noise) if base else spread * noise
        out[name] = jnp.asarray(drawn.astype(out[name].dtype))
    for name, factor in factors.items():
        out[name] = (out[name] * factor).astype(out[name].dtype)
    return out
```

```python
from contextlib import ExitStack

import concourse.bass as bass
from concourse import mybir

P = 128
SLOTS = 4
SKIP = 1 << 22
FMAX = 3.4028234663852886e38

ALU = mybir.AluOpType
F32 = mybir.dt.float32
I32 = mybir.dt.int32
AX_X = mybir.AxisListType.X


def build_embedding_bag(nc, ids, lengths, tables, out):
    B, F, L = ids.shape
    _, V, E = tables.shape
    BLOCKS = B // P
    TILES = BLOCKS * F
    STEPS = TILES // SLOTS
    assert B % P == 0 and F % SLOTS == 0 and F * V + SKIP < 1 << 24

    table_rows = tables.rearrange("f v e -> (f v) e")
    ids_rows = ids.rearrange("(k p) f l -> p k (f l)", p=P)
    length_rows = lengths.rearrange("(k p) f -> p k f", p=P)
    out_rows = out.rearrange("(k p) n -> k p n", p=P)

    with ExitStack() as ctx:
        def sb(name, shape, dt):
            return ctx.enter_context(nc.sbuf_tensor(name, shape, dt))

        def sem(name):
            return ctx.enter_context(nc.semaphore(name))

        id_tile = sb("id_tile", [P, BLOCKS, F * L], I32)
        len_tile = sb("len_tile", [P, BLOCKS, F], I32)
        first_row = sb("first_row", [P, F, L], I32)
        position = sb("position", [P, F, L], I32)
        masked = sb("masked", [P, F, L], I32)
        row_of = sb("row_of", [P, TILES, L], I32)
        row_now = sb("row_now", [P, SLOTS, L], I32)
        rows = sb("rows", [P, SLOTS, L * E], F32)
        pooled = sb("pooled", [P, BLOCKS, F * E], F32)
        clamped = sb("clamped", [P, F * E], F32)
        is_number = sb("is_number", [P, F * E], I32)
        result = sb("result", [P, BLOCKS, F * E], F32)

        ids_in = sem("ids_in")
        lengths_in = sem("lengths_in")
        iotas_done = sem("iotas_done")
        index_step = sem("index_step")
        buffer_ready = [sem(f"buffer_ready{s}") for s in range(SLOTS)]
        rows_in = [sem(f"rows_in{s}") for s in range(SLOTS)]
        fill_begun = sem("fill_begun")
        pooled_done = sem("pooled_done")
        clean_step = sem("clean_step")
        block_done = sem("block_done")
        stored = sem("stored")

        block = ctx.enter_context(nc.Block())

        @block.sync
        def _(sp):
            sp.dma_start(id_tile[:], ids_rows).then_inc(ids_in, 16)
            sp.dma_start(len_tile[:], length_rows).then_inc(lengths_in, 16)
            for k in range(BLOCKS):
                sp.wait_ge(block_done, k + 1)
                sp.dma_start(out_rows[k], result[:, k, :]).then_inc(stored, 16)
            sp.wait_ge(stored, 16 * BLOCKS)

        @block.gpsimd
        def _(pool):
            nc.gpsimd.iota(first_row[:], pattern=[[V, F], [0, L]], base=0, channel_multiplier=0).then_inc(iotas_done, 1)
            nc.gpsimd.iota(position[:], pattern=[[0, F], [1, L]], base=0, channel_multiplier=0).then_inc(iotas_done, 1)
            last_row = pool.to_reg(F * V - 1)
            with pool.Fori(0, STEPS) as step:
                for s in range(SLOTS):
                    pool.wait_ge(buffer_ready[s], step + 1)
                    pool.sem_inc(fill_begun, 1)
                    for l in range(L):
                        nc.gpsimd.indirect_dma_start(
                            out=rows[:, s, l * E:(l + 1) * E], out_offset=None, in_=table_rows,
                            in_offset=bass.IndirectOffsetOnAxis(ap=row_now[:, s, l:l + 1], axis=0),
                            bounds_check=last_row, oob_is_err=False).then_inc(rows_in[s], 16)

        @block.vector
        def _(dve):
            dve.wait_ge(iotas_done, 2)
            dve.wait_ge(ids_in, 16)
            dve.wait_ge(lengths_in, 16)
            n = 0
            for k in range(BLOCKS):
                idx = row_of[:, k * F:(k + 1) * F, :]
                lens = len_tile[:, k, :].unsqueeze(2).to_broadcast([P, F, L])
                nc.vector.tensor_tensor(masked[:], position[:], lens, ALU.is_ge).then_inc(index_step, 1)
                nc.vector.tensor_tensor(idx, id_tile[:, k, :].rearrange("p (f l) -> p f l", l=L), first_row[:],
                                        ALU.add).then_inc(index_step, 1)
                n += 2
                dve.wait_ge(index_step, n)
                nc.vector.scalar_tensor_tensor(out=idx, in0=masked[:], scalar=float(SKIP), in1=idx,
                                               op0=ALU.mult, op1=ALU.add).then_inc(index_step, 1)
                n += 1
                dve.wait_ge(index_step, n)
            for s in range(SLOTS):
                nc.vector.memset(rows[:, s, :], 0.0).then_inc(index_step, 1)
                n += 1
                dve.wait_ge(index_step, n)
                nc.vector.tensor_copy(row_now[:, s, :], row_of[:, s, :]).then_inc(buffer_ready[s], 1)

            def pool_tile(step, s):
                t = step * SLOTS + s
                dve.wait_ge(rows_in[s], (step + 1) * 16 * L)
                nc.vector.tensor_reduce(
                    out=pooled[:].rearrange("p k (f e) -> p (k f) e", e=E)[:, bass.ds(t, 1), :].rearrange("p a e -> p (a e)"),
                    in_=rows[:, s, :].rearrange("p (l e) -> p e l", e=E), axis=AX_X, op=ALU.add).then_inc(pooled_done, 1)
                dve.wait_ge(pooled_done, t + 1)

            with dve.Fori(0, STEPS - 1) as step:
                for s in range(SLOTS):
                    pool_tile(step, s)
                    nc.vector.memset(rows[:, s, :], 0.0).then_inc(index_step, 1)
                    dve.wait_ge(index_step, step * SLOTS + (n + s + 1))
                    nc.vector.tensor_copy(row_now[:, s, :],
                                          row_of[:, bass.ds((step + 1) * SLOTS + s, 1), :].rearrange("p a l -> p (a l)")
                                          ).then_inc(buffer_ready[s], 1)
            for s in range(SLOTS):
                pool_tile(STEPS - 1, s)
            c = 0
            for k in range(BLOCKS):
                nc.vector.memset(result[:, k, :], 0.0).then_inc(clean_step, 1)
                nc.vector.tensor_scalar(clamped[:], pooled[:, k, :], FMAX, -FMAX, ALU.min, ALU.max).then_inc(clean_step, 1)
                nc.vector.tensor_tensor(is_number[:], pooled[:, k, :], pooled[:, k, :], ALU.is_equal).then_inc(clean_step, 1)
                c += 3
                dve.wait_ge(clean_step, c)
                nc.vector.copy_predicated(result[:, k, :], is_number[:], clamped[:]).then_inc(block_done, 1)
                dve.wait_ge(block_done, k + 1)


_INS = ["r_ids", "r_lengths", "L0_rec_tables"]


def kernel(**inputs):
    import numpy as _np
    import concourse.bacc as _bacc
    from concourse import mybir as _mybir
    from concourse.bass_utils import run_bass_kernel_spmd as _run

    nc = _bacc.Bacc("TRN2", target_bir_lowering=False, num_devices=1)
    arrays, args = {}, []
    for name in _INS:
        a = _np.ascontiguousarray(inputs[name])
        arrays[f"in_{name}_dram"] = a
        args.append(nc.dram_tensor(f"in_{name}_dram", a.shape, _mybir.dt.from_np(a.dtype), kind="ExternalInput").ap())
    B, F, _ = inputs["r_ids"].shape
    E = inputs["L0_rec_tables"].shape[2]
    out = nc.dram_tensor("out_0_dram", (B, F * E), _mybir.dt.float32, kind="ExternalOutput").ap()
    build_embedding_bag(nc, *args, out)
    r = _run(nc, [arrays], core_ids=[0])
    return r.results[0]["out_0_dram"]
```

```python
from contextlib import ExitStack

import concourse.bass as bass
from concourse import mybir

P = 128
M = 20
ROUNDS = 4
TRIO = 3
GROUP = 2 * TRIO
SETS = 3
PARTS = 3
CHUNKS = 7
PER_CHUNK = 6
SLOTS = 3
CLEAN = 128
LAG = 3
SKIP = 1 << 22
FMAX = 3.4028234663852886e38
MAGIC = 12582912.0

ALU = mybir.AluOpType
ACT = mybir.ActivationFunctionType
F32 = mybir.dt.float32
F16 = mybir.dt.float16
BF16 = mybir.dt.bfloat16
I32 = mybir.dt.int32
U8 = mybir.dt.uint8
AX_X = mybir.AxisListType.X


def geometry(B, V):
    J = -(-V // P)
    HALF = B // 2
    return J, HALF, 1 + CHUNKS * PER_CHUNK


def build_embedding_bag(nc, ids, lengths, tables, lookup_ids, lookup_lengths, lookup_place, ramps, out):
    B, F, L = ids.shape
    _, V, E = tables.shape
    J, HALF, GROUPS = geometry(B, V)
    G = F - M
    BLOCKS = B // P
    FPR = M // ROUNDS
    PHASES = 2 * FPR
    WIDE = J * TRIO
    JC = J // CHUNKS
    CE = JC * E
    PADDED = GROUPS * GROUP
    PIECES = G * E // CLEAN
    assert BLOCKS == ROUNDS and M % ROUNDS == 0 and J % CHUNKS == 0 and JC % 2 == 0 and G % SLOTS == 0
    assert PADDED >= HALF and TRIO * L <= 64 and WIDE <= 512 and HALF == 2 * P and 2 * PARTS * E <= 512
    assert (M - 1) * V + J * P <= F * V and F * V + SKIP < 1 << 24

    table_rows = tables.rearrange("f v e -> (f v) e")
    out_rows = out.rearrange("(k p) n -> k p n", p=P)
    half_rows = out.rearrange("(h k p) n -> h p k n", h=2, p=P)

    with ExitStack() as ctx:
        def sb(name, shape, dt):
            return ctx.enter_context(nc.sbuf_tensor(name, shape, dt))

        def psum(name, shape, dt):
            return ctx.enter_context(nc.psum_tensor(name, shape, dt))

        def sem(name):
            return ctx.enter_context(nc.semaphore(name))

        counts = [sb(f"counts{h}", [P, J, PADDED], BF16) for h in range(2)]
        table = sb("table", [P, PARTS, J * E], F32)
        onehot_p = sb("onehot_p", [P, PER_CHUNK + 1, P], BF16)
        onehot_j = sb("onehot_j", [P, PER_CHUNK + 1, WIDE], BF16)
        ramp = sb("ramp", [P, P + WIDE], F16)
        place = sb("place", [P, 2], F32)
        p_of = sb("p_of", [P, M * 2 * GROUPS], U8)
        j_of = sb("j_of", [P, M * 2 * GROUPS], F16)
        clean = sb("clean", [P, 2, 2 * E], F32)
        row_of = sb("row_of", [P, BLOCKS * G + SLOTS, L], I32)
        row_now = sb("row_now", [P, SLOTS, L], I32)
        rows = sb("rows", [P, SLOTS, L * E], F32)
        gathered = sb("gathered", [P, G * E], F32)
        zero = sb("zero", [P, 1], F32)
        is_nan = sb("is_nan", [P, CLEAN], I32)

        N = M * 2 * GROUPS
        scratch = counts[1][:].rearrange("p a b -> p (a b)").bitcast(I32)
        at = [0]

        def piece(n, dt=I32):
            at[0] += n
            v = scratch[:, at[0] - n:at[0]]
            return v if dt == I32 else v.bitcast(dt)

        look_id, look_len = piece(N), piece(N)
        work_a, work_b = piece(N, F32), piece(N, F32)
        id_tile = piece(BLOCKS * G * L).rearrange("p (k n) -> p k n", k=BLOCKS)
        len_tile = piece(BLOCKS * G).rearrange("p (k n) -> p k n", k=BLOCKS)
        first_row = piece(G * L).rearrange("p (f l) -> p f l", l=L)
        position = piece(G * L).rearrange("p (f l) -> p f l", l=L)
        masked = piece(G * L).rearrange("p (f l) -> p f l", l=L)

        pairs = [psum(f"pairs{s}", [P, 2, 512], F32) for s in range(SETS)]
        sums = [psum(f"sums{h}", [P, 512], F32) for h in range(2)]

        inputs_in = sem("inputs_in")
        lookups_in = sem("lookups_in")
        gather_in = sem("gather_in")
        iotas_done = sem("iotas_done")
        table_in = [sem(f"table_in{c}") for c in range(CHUNKS)]
        table_landed = sem("table_landed")
        onehots_ready = sem("onehots_ready")
        counted = sem("counted")
        counts_saved = sem("counts_saved")
        rest_done = sem("rest_done")
        parts_ready = sem("parts_ready")
        table_used = sem("table_used")
        sums_done = sem("sums_done")
        sums_read = sem("sums_read")
        cleaned = sem("cleaned")
        stored = [sem(f"stored{h}") for h in range(2)]
        vec = sem("vec")
        clean_step = sem("clean_step")
        clean_checked = sem("clean_checked")
        buffer_ready = [sem(f"buffer_ready{s}") for s in range(SLOTS)]
        fill_begun = sem("fill_begun")
        rows_in = [sem(f"rows_in{s}") for s in range(SLOTS)]
        added = sem("added")
        gathered_ready = sem("gathered_ready")
        gathered_stored = sem("gathered_stored")

        def group(rnd, ph, c, i):
            return rnd * (PHASES * GROUPS) + c * PER_CHUNK + (ph * GROUPS + i + 1)

        def pair(ph, i):
            return pairs[(ph + i + 1) % SETS]

        def added_at(place):
            return [t for t in range(G) if t * 2 * PHASES // G == place]

        def known(n, below):
            return isinstance(n, int) and n < below

        block = ctx.enter_context(nc.Block())

        @block.sync
        def _(sp):
            sp.dma_start(look_id, lookup_ids).then_inc(lookups_in, 16)
            sp.dma_start(look_len, lookup_lengths).then_inc(lookups_in, 16)
            sp.dma_start(ramp[:], ramps).then_inc(inputs_in, 16)
            sp.dma_start(place[:], lookup_place).then_inc(inputs_in, 16)

            def load(f, c, wait=True):
                if wait and c == CHUNKS - 1:
                    sp.wait_ge(sums_done, 2 * f)
                elif wait:
                    sp.wait_ge(table_used, (f - 1) * (CHUNKS - 1) + (c + 1))
                src = table_rows[bass.ds(f * V, J * P), :].rearrange("(p j) e -> p (j e)", j=J)
                sp.dma_start(table[:, 0, c * CE:(c + 1) * CE], src[:, c * CE:(c + 1) * CE]).then_inc(table_in[c], 16)

            def report(f, c):
                sp.wait_ge(table_in[c], f * 16 + 16)
                sp.sem_inc(table_landed, 1)

            def store(f, h):
                sp.wait_ge(cleaned, 2 * f + (h + 1))
                dst = half_rows[h][:, :, bass.ds(f * E, E)]
                sp.dma_start(dst, clean[:, h, :].rearrange("p (k e) -> p k e", e=E)).then_inc(stored[h], 16)

            for c in range(CHUNKS):
                load(0, c, wait=False)
            for c in range(CHUNKS):
                report(0, c)
            with sp.Fori(1, M) as f:
                for c in range(CHUNKS):
                    load(f, c)
                    if c:
                        report(f, c - 1)
                report(f, CHUNKS - 1)
                store(f - 1, 0)
                store(f - 1, 1)
            store(M - 1, 0)
            store(M - 1, 1)
            for h in range(2):
                sp.wait_ge(stored[h], 16 * M)

        @block.gpsimd
        def _(pool):
            nc.gpsimd.iota(first_row, pattern=[[V, G], [0, L]], base=M * V, channel_multiplier=0).then_inc(iotas_done, 1)
            nc.gpsimd.iota(position, pattern=[[0, G], [1, L]], base=0, channel_multiplier=0).then_inc(iotas_done, 1)
            last_row = pool.to_reg(F * V - 1)
            with pool.Fori(0, ROUNDS) as rnd:
                for t in range(G):
                    s = t % SLOTS
                    pool.wait_ge(buffer_ready[s], rnd * (G // SLOTS) + (t // SLOTS + 1))
                    pool.sem_inc(fill_begun, 1)
                    for l in range(L):
                        nc.gpsimd.indirect_dma_start(
                            out=rows[:, s, l * E:(l + 1) * E], out_offset=None, in_=table_rows,
                            in_offset=bass.IndirectOffsetOnAxis(ap=row_now[:, s, l:l + 1], axis=0),
                            bounds_check=last_row, oob_is_err=False).then_inc(rows_in[s], 16)

        @block.scalar
        def _(act):
            ids_rows = ids[:, M:F, :].rearrange("(k p) f l -> p k (f l)", p=P)
            len_rows = lengths[:, M:F].rearrange("(k p) f -> p k f", p=P)
            act.dma_start(id_tile, ids_rows).then_inc(gather_in, 16)
            act.dma_start(len_tile, len_rows).then_inc(gather_in, 16)

            def save_counts(rnd, ph, c, i):
                g = PER_CHUNK * c + (i + 1)
                act.wait_ge(counted, group(rnd, ph, c, i) + 1)
                dst = counts[ph % 2][:, :, bass.ds(g * GROUP, GROUP)].rearrange("p j (t b) -> p t j b", t=2)
                src = pair(ph, i)[:, :, 0:WIDE].rearrange("p t (j b) -> p t j b", b=TRIO)
                nc.scalar.activation(dst, src, ACT.Copy).then_inc(counts_saved, 1)

            def store_gathered(rnd):
                act.wait_ge(gathered_ready, rnd * PIECES + PIECES)
                dst = out_rows[bass.ds(rnd, 1), :, M * E:F * E].rearrange("a p n -> (a p) n")
                act.dma_start(dst, gathered[:]).then_inc(gathered_stored, 16)

            def refill(rnd, t):
                s = t % SLOTS
                k = rnd * G + t
                act.wait_ge(added, k + 1)
                nc.scalar.activation(rows[:, s, :], zero[:].to_broadcast([P, L * E]), ACT.Copy)
                nc.scalar.activation(row_now[:, s, :], row_of[:, bass.ds(k + SLOTS, 1), :].rearrange("p a l -> p (a l)"),
                                     ACT.Copy).then_inc(buffer_ready[s], 1)

            def round_(rnd, first):
                for ph in range(PHASES):
                    save_counts(rnd, ph, 0, -1)
                    if ph == 0 and not first:
                        store_gathered(rnd - 1)
                    for lo, hi in ((0, 1), (1, LAG + 1), (LAG + 1, CHUNKS)):
                        with act.Fori(lo, hi) as c:
                            for i in range(PER_CHUNK):
                                save_counts(rnd, ph, c, i)
                        if hi < CHUNKS and not (first and ph == 0 and lo == 0):
                            for t in added_at(2 * ph - (lo == 0)):
                                refill(rnd, t)
                for t in added_at(2 * PHASES - 1):
                    refill(rnd, t)

            round_(0, True)
            with act.Fori(1, ROUNDS) as rnd:
                round_(rnd, False)
            store_gathered(ROUNDS - 1)
            act.wait_ge(gathered_stored, 16 * ROUNDS)

        @block.tensor
        def _(pe):
            def count(rnd, ph, c, i):
                n = group(rnd, ph, c, i)
                pe.wait_ge(onehots_ready, n + 1)
                free = n if ph == 0 and i == -1 else n - (SETS - 1)
                if not known(free, 1):
                    pe.wait_ge(counts_saved, free)
                for t in range(2):
                    last = nc.tensor.matmul(pair(ph, i)[:, t, 0:WIDE], onehot_p[64 * t:64 * t + 64, i + 1, :],
                                            onehot_j[64 * t:64 * t + 64, i + 1, :], start=True, stop=True)
                last.then_inc(counted, 1)

            parts = table[:].bitcast(BF16).rearrange("p t (j e x) -> p t j e x", e=E, x=2)

            def multiply(h, j0, j1):
                for j in range(j0, j1):
                    for k in range(HALF // P):
                        last = nc.tensor.matmul(sums[h][:, k * PARTS * E:(k + 1) * PARTS * E],
                                                counts[h][:, j, k * P:(k + 1) * P], parts[:, :, j, :, 1],
                                                start=(j == 0 and k == 0), stop=(j == J - 1), skip_group_check=True)
                if j1 == J:
                    last.then_inc(sums_done, 1)
                elif h == 1 and j1 % JC == 0:
                    last.then_inc(table_used, 1)

            def phase(rnd, ph, with_counts=True, with_products=True):
                q = rnd * PHASES + ph
                h = (ph - 1) % 2
                if with_counts:
                    count(rnd, ph, 0, -1)
                if with_products:
                    pe.wait_ge(counts_saved, rnd * (PHASES * GROUPS) + ph * GROUPS)
                    if not known(q, 3):
                        pe.wait_ge(sums_read, q - 2)
                for c in range(CHUNKS):
                    for i in range(PER_CHUNK):
                        if with_counts:
                            count(rnd, ph, c, i)
                        if with_products and h == 0 and i == 0:
                            pe.wait_ge(parts_ready, rnd * (FPR * CHUNKS) + ((ph - 1) // 2 * CHUNKS + c + 1))
                        if with_products:
                            multiply(h, c * JC + i * JC // PER_CHUNK, c * JC + (i + 1) * JC // PER_CHUNK)

            for ph in range(PHASES):
                phase(0, ph, with_products=ph >= 1)
            with pe.Fori(1, ROUNDS) as rnd:
                for ph in range(PHASES):
                    phase(rnd, ph)
            phase(ROUNDS, 0, with_counts=False)

        @block.vector
        def _(dve):
            n = [0]

            def step(ins):
                n[0] += 1
                ins.then_inc(vec, 1)
                dve.wait_ge(vec, n[0])

            nc.vector.memset(zero[:], 0.0)
            nc.vector.memset(row_of[:, BLOCKS * G:, :], 0)
            for s in range(SLOTS):
                nc.vector.memset(rows[:, s, :], 0.0)
            dve.wait_ge(iotas_done, 2)
            dve.wait_ge(gather_in, 32)
            for k in range(BLOCKS):
                idx = row_of[:, k * G:(k + 1) * G, :]
                lens = len_tile[:, k, :].unsqueeze(2).to_broadcast([P, G, L])
                nc.vector.tensor_tensor(masked, position, lens, ALU.is_ge)
                step(nc.vector.tensor_tensor(idx, id_tile[:, k, :].rearrange("p (f l) -> p f l", l=L), first_row, ALU.add))
                step(nc.vector.scalar_tensor_tensor(out=idx, in0=masked, scalar=float(SKIP), in1=idx,
                                                    op0=ALU.mult, op1=ALU.add))
                if k == 0:
                    for s in range(SLOTS):
                        nc.vector.tensor_copy(row_now[:, s, :], row_of[:, s, :]).then_inc(buffer_ready[s], 1)
            dve.wait_ge(inputs_in, 32)
            dve.wait_ge(lookups_in, 32)
            step(nc.vector.tensor_scalar(work_a, look_id, 1.0 / J, 0.5 / J - 0.5, ALU.mult, ALU.add))
            step(nc.vector.tensor_scalar(p_of[:], work_a, MAGIC, MAGIC, ALU.add, ALU.subtract))
            step(nc.vector.scalar_tensor_tensor(out=work_b, in0=p_of[:], scalar=-float(J), in1=look_id,
                                                op0=ALU.mult, op1=ALU.add))
            step(nc.vector.tensor_scalar(work_a, work_b, float(TRIO), place[:, 1:2], ALU.mult, ALU.add))
            step(nc.vector.scalar_tensor_tensor(out=j_of[:], in0=look_len, scalar=place[:, 0:1], in1=work_a,
                                                op0=ALU.is_gt, op1=ALU.mult))

            def onehots(rnd, ph, c, i):
                n = group(rnd, ph, c, i)
                if not known(n - (PER_CHUNK - 1), 1):
                    dve.wait_ge(counted, n - (PER_CHUNK - 1))
                nc.vector.tensor_scalar(onehot_p[:, i + 1, :], ramp[:, 0:P], p_of[:, bass.ds(n, 1)], None, ALU.is_equal)
                nc.vector.tensor_scalar(onehot_j[:, i + 1, :], ramp[:, P:], j_of[:, bass.ds(n, 1)], None,
                                        ALU.is_equal).then_inc(onehots_ready, 1)

            high_of_table = table[:, 0, :].bitcast(BF16).rearrange("p (n x) -> p n x", x=2)[:, :, 1]
            high_of_rest = table[:, 1, :].bitcast(BF16).rearrange("p (n x) -> p n x", x=2)[:, :, 1]

            def cut_rest(f, c):
                sl = bass.ds(c * CE, CE)
                dve.wait_ge(table_landed, f * CHUNKS + c + 1)
                nc.vector.tensor_tensor(table[:, 1, sl], table[:, 0, sl], high_of_table[:, sl],
                                        ALU.subtract).then_inc(rest_done, 1)

            def cut_low(f, c):
                sl = bass.ds(c * CE, CE)
                dve.wait_ge(rest_done, f * CHUNKS + c + 1)
                nc.vector.tensor_tensor(table[:, 2, sl], table[:, 1, sl], high_of_rest[:, sl],
                                        ALU.subtract).then_inc(parts_ready, 1)

            def cleaning(dst, src, k):
                w = dst.shape[1]
                nc.vector.tensor_tensor(is_nan[:, 0:w], src, src, ALU.not_equal).then_inc(clean_step, 1)
                nc.vector.tensor_scalar(dst, src, FMAX, -FMAX, ALU.min, ALU.max).then_inc(clean_step, 1)
                dve.wait_ge(clean_step, k * 2 + 2)
                dve.sem_inc(clean_checked, 1)
                return nc.vector.copy_predicated(dst, is_nan[:, 0:w], zero[:].to_broadcast([P, w]))

            def clean_half(rnd, ph):
                q = rnd * PHASES + (ph - 2)
                h = ph % 2
                if not known(q, 1):
                    dve.wait_ge(cleaned, q)
                dve.wait_ge(sums_done, q + 1)
                f = rnd * FPR + (ph // 2 - 1)
                if not known(f, 1):
                    dve.wait_ge(stored[h], f * 16)
                nc.vector.tensor_reduce(
                    out=clean[:, h, :].rearrange("p (k e) -> p k e", e=E),
                    in_=sums[h][:, 0:2 * PARTS * E].rearrange("p (k t e) -> p k e t", t=PARTS, e=E),
                    axis=AX_X, op=ALU.add).then_inc(sums_read, 1)
                dve.wait_ge(sums_read, q + 1)
                cleaning(clean[:, h, :], clean[:, h, :], q + rnd * PIECES).then_inc(cleaned, 1)

            def clean_gathered(rnd):
                dve.wait_ge(cleaned, rnd * PHASES + (PHASES - 2))
                for m in range(PIECES):
                    sl = slice(m * CLEAN, (m + 1) * CLEAN)
                    if m:
                        dve.wait_ge(gathered_ready, rnd * PIECES + m)
                    cleaning(gathered[:, sl], gathered[:, sl],
                             rnd * (PHASES + PIECES) + (PHASES - 2 + m)).then_inc(gathered_ready, 1)

            def add_rows(rnd, t):
                s = t % SLOTS
                k = rnd * G + t
                if t == 0 and not known(rnd, 1):
                    dve.wait_ge(gathered_stored, rnd * 16)
                dve.wait_ge(rows_in[s], rnd * (G // SLOTS * 16 * L) + (t // SLOTS + 1) * 16 * L)
                nc.vector.tensor_reduce(out=gathered[:, t * E:(t + 1) * E],
                                        in_=rows[:, s, :].rearrange("p (l e) -> p e l", e=E),
                                        axis=AX_X, op=ALU.add).then_inc(added, 1)

            def chunk(rnd, ph, c, cut):
                f = rnd * FPR + ph // 2
                for i in range(PER_CHUNK):
                    onehots(rnd, ph, c, i)
                    if cut is not None and i == 0:
                        cut_rest(f, c + cut)
                    if cut is not None and i == 3:
                        cut_low(f, c + cut)

            def round_(rnd, first):
                for ph in range(PHASES):
                    onehots(rnd, ph, 0, -1)
                    for lo, hi in ((0, LAG), (LAG, CHUNKS)):
                        cut = {(0, LAG): -LAG, (1, 0): CHUNKS - LAG}.get((ph % 2, lo))
                        if first and ph == 0 and lo == 0:
                            for c in range(lo, hi):
                                chunk(rnd, ph, c, cut)
                        else:
                            with dve.Fori(lo, hi) as c:
                                chunk(rnd, ph, c, cut)
                        for t in added_at(2 * ph + (lo > 0)):
                            add_rows(rnd, t)
                        if lo == 0 and not (first and ph < 2):
                            clean_half(rnd, ph)
                clean_gathered(rnd)

            round_(0, True)
            with dve.Fori(1, ROUNDS) as rnd:
                round_(rnd, False)
            clean_half(ROUNDS, 0)
            clean_half(ROUNDS, 1)


def kernel(r_ids, r_lengths, L0_rec_tables):
    import numpy as np
    import concourse.bacc as bacc
    from concourse.bass_utils import run_bass_kernel_spmd

    ids, lengths, tables = (np.ascontiguousarray(a) for a in (r_ids, r_lengths, L0_rec_tables))
    B, F, L = ids.shape
    _, V, E = tables.shape
    J, HALF, GROUPS = geometry(B, V)

    def by_group(a):
        padded = np.zeros((2, GROUPS * GROUP, M, L), a.dtype)
        padded[:, :HALF] = a.reshape(2, HALF, M, L)
        there = np.zeros((2, 64, M, 2, GROUPS), a.dtype)
        there[:, :TRIO * L] = padded.reshape(2, GROUPS, 2, TRIO, M, L).transpose(2, 3, 5, 4, 0, 1).reshape(
            2, TRIO * L, M, 2, GROUPS)
        return there.reshape(P, M * 2 * GROUPS)

    place = np.zeros((2, 64, 2), np.float32)
    place[:, :, 0] = 1 << 20
    place[:, :TRIO * L, 0] = np.arange(TRIO * L) % L
    place[:, :TRIO * L, 1] = 1 + np.arange(TRIO * L) // L
    ramps = np.concatenate([np.arange(P), 1 + np.arange(J * TRIO)]).astype(np.float16)
    arrays = {
        "ids": ids,
        "lengths": lengths,
        "tables": tables,
        "lookup_ids": by_group(ids[:, :M]),
        "lookup_lengths": by_group(np.broadcast_to(lengths[:, :M, None], (B, M, L))),
        "lookup_place": place.reshape(P, 2),
        "ramps": np.tile(ramps, (P, 1)),
    }
    nc = bacc.Bacc("TRN2", target_bir_lowering=False, num_devices=1)
    args = [nc.dram_tensor(n, a.shape, mybir.dt.from_np(a.dtype), kind="ExternalInput").ap()
            for n, a in arrays.items()]
    out = nc.dram_tensor("out", (B, F * E), F32, kind="ExternalOutput").ap()
    build_embedding_bag(nc, *args, out)
    return run_bass_kernel_spmd(nc, [arrays], core_ids=[0]).results[0]["out"]
```

```python
from contextlib import ExitStack

import concourse.bass as bass
from concourse import mybir

P = 128
M = 15
TRIO = 3
GROUP = 2 * TRIO
SETS = 3
PARTS = 3
CHUNKS = 7
PER_CHUNK = 6
LAG = 3
SLOW = 2
BUFFERS = 4
FIFTH = (0, 2, 1, 3, 4)
UP = (True, True, False, False, True)
BUFFER = (0, 1, 0, 2, 3)
SLOTS = len(BUFFER)
BEGIN = 2
EARLY = 1
NEXT = ((2, 0), (1, 1), (0, 1), (3, 1), (4, 1))
SKIP = 1 << 22
DMA_SCRATCH = 15 * 1024
FMAX = 3.4028234663852886e38
MAGIC = 12582912.0

ALU = mybir.AluOpType
ACT = mybir.ActivationFunctionType
F32 = mybir.dt.float32
F16 = mybir.dt.float16
BF16 = mybir.dt.bfloat16
I32 = mybir.dt.int32
U8 = mybir.dt.uint8
AX_X = mybir.AxisListType.X


def geometry(B, V):
    J = -(-V // P)
    HALF = B // 2
    return J, HALF, 1 + CHUNKS * PER_CHUNK


def build_embedding_bag(nc, ids, lengths, tables, lookup_ids, lookup_lengths, lookup_place, ramps, triangle,
                        out_counted, out_gathered):
    B, F, L = ids.shape
    _, V, E = tables.shape
    J, HALF, GROUPS = geometry(B, V)
    G = F - M
    BLOCKS = B // P
    TILES = BLOCKS * G
    RANKS = TILES * P
    RECORD = L + 1
    WIDE = J * TRIO
    JC = J // CHUNKS
    CE = JC * E
    PADDED = GROUPS * GROUP
    N = M * 2 * GROUPS
    FULL, EXTRA = TILES // SLOTS, TILES % SLOTS
    TAKES = [FULL + (1 if k < EXTRA else 0) for k in range(SLOTS)]
    by_fifth = sorted(range(SLOTS), key=lambda k: FIFTH[k])
    FIRST = [sum(TAKES[m] for m in by_fifth[:FIFTH[k]]) for k in range(SLOTS)]
    COLUMN = [sum(TAKES[:k]) for k in range(SLOTS)]
    assert 0 < EXTRA and EXTRA >= EARLY and M - 2 <= FULL <= M and J % CHUNKS == 0 and PADDED >= HALF
    assert TRIO * L <= 64 and WIDE <= 512 and HALF == 2 * P and 2 * PARTS * E <= 512
    assert (M - 1) * V + J * P <= F * V and F * V + SKIP < 1 << 24

    table_rows = tables.rearrange("f v e -> (f v) e")
    sorted_records = nc.dram_tensor("sorted_records", (RANKS, RECORD), I32, kind="Internal").ap()
    counted_rows = out_counted.rearrange("(m p) n -> p m n", p=P)

    with ExitStack() as ctx:
        def sb(name, shape, dt):
            return ctx.enter_context(nc.sbuf_tensor(name, shape, dt))

        def psum(name, shape, dt):
            return ctx.enter_context(nc.psum_tensor(name, shape, dt))

        def sem(name):
            return ctx.enter_context(nc.semaphore(name))

        counts = [sb(f"counts{h}", [P, J, PADDED], BF16) for h in range(2)]
        table = sb("table", [P, PARTS, J * E], F32)
        onehot_p = sb("onehot_p", [P, PER_CHUNK // 2 + 1, P, 2], BF16)
        onehot_j = sb("onehot_j", [P, PER_CHUNK + 1, WIDE], BF16)
        ramp = sb("ramp", [P, 2 * P + WIDE], F16)
        place = sb("place", [P, 2], F32)
        p_of = sb("p_of", [P, N], U8)
        p_now = sb("p_now", [P, 2, GROUPS], F16)
        j_of = sb("j_of", [P, N], F16)
        pooled = sb("pooled", [P, BLOCKS * E], F32)
        row_now = sb("row_now", [P, BUFFERS, RECORD], I32)
        rows = sb("rows", [P, BUFFERS, L * E], F32)
        summed = sb("summed", [P, SLOTS * E], F32)
        place_summed = sb("place_summed", [P, SLOTS], I32)
        gathered = sb("gathered", [P, SLOTS * E], F32)
        place_now = sb("place_now", [P, SLOTS], I32)
        depth = sb("depth", [P, TILES], I32)
        arrival = sb("arrival", [P, TILES], I32)
        zero = sb("zero", [P, 1], F32)
        is_nan = sb("is_nan", [P, max(BLOCKS, SLOTS) * E], U8)

        rank = summed[:].bitcast(I32)[:, 0:TILES]

        FIRST_COLUMNS = slice(0, 2 * GROUPS)
        OTHER_COLUMNS = slice(2 * GROUPS, N)

        scratch = counts[1][:].rearrange("p a b -> p (a b)").bitcast(I32)
        at = [0]

        def piece(n, dt=I32):
            at[0] += n
            v = scratch[:, at[0] - n:at[0]]
            return v if dt == I32 else v.bitcast(dt)

        look_id, look_len = piece(N), piece(N)
        work_a, work_b = piece(N, F32), piece(N, F32)
        id_tile = piece(TILES * L).rearrange("p (k n) -> p k n", k=BLOCKS)
        len_tile = piece(TILES)
        first_row = piece(G * L).rearrange("p (f l) -> p f l", l=L)
        position = piece(G * L).rearrange("p (f l) -> p f l", l=L)
        masked = piece(G * L).rearrange("p (f l) -> p f l", l=L)
        value = piece(L + 1)
        last_rank = piece(TILES)
        length = piece(TILES, F32)
        has = piece((L + 1) * TILES, F32)
        until = piece((L + 1) * TILES, F32)
        before = piece(L + 1, F32)
        shift = piece(L + 1, F32)
        below = piece(L + 1, F32)
        rank_f, depth_f, arrival_f = piece(TILES, F32), piece(TILES, F32), piece(TILES, F32)
        halves = piece(P + L + 1).bitcast(F16)
        tri, has_sum, before_h = halves[:, 0:2 * P], halves[:, 2 * P:2 * P + L + 1], halves[:, 2 * P + L + 1:2 * (P + L + 1)]
        record_words = rows[:].rearrange("p s n -> p (s n)").bitcast(I32)[:, (BUFFERS * L * E - TILES * RECORD):]
        records = record_words.rearrange("p (t w) -> p t w", w=RECORD)

        pairs = [psum(f"pairs{s}", [P, 2, 512], F32) for s in range(SETS)]
        sums = [psum(f"sums{h}", [P, 512], F32) for h in range(2)]

        ramps_in = sem("ramps_in")
        first_lookups_in = sem("first_lookups_in")
        other_lookups_in = sem("other_lookups_in")
        gather_ids_in = sem("gather_ids_in")
        iotas_done = sem("iotas_done")
        prepared = sem("prepared")
        table_in = [sem(f"table_in{c}") for c in range(CHUNKS)]
        table_landed = sem("table_landed")
        rest_done = sem("rest_done")
        parts_ready = sem("parts_ready")
        table_used = sem("table_used")
        onehots_ready = sem("onehots_ready")
        counted = sem("counted")
        counts_saved = sem("counts_saved")
        sums_done = sem("sums_done")
        sums_read = sem("sums_read")
        p_now_ready = sem("p_now_ready")
        clean_step = sem("clean_step")
        waited = sem("waited")
        pooled_ready = sem("pooled_ready")
        pooled_stored = sem("pooled_stored")
        pooled_free = sem("pooled_free")
        lengths_in = sem("lengths_in")
        length_counts = sem("length_counts")
        ranked = sem("ranked")
        records_ready = sem("records_ready")
        records_out = sem("records_out")
        rows_zeroed = sem("rows_zeroed")
        records_gone = sem("records_gone")
        first_rows_in = sem("first_rows_in")
        depths_ready = sem("depths_ready")
        buffer_zeroed = [sem(f"buffer_zeroed{s}") for s in range(SLOTS)]
        row_now_in = [sem(f"row_now_in{s}") for s in range(SLOTS)]
        gathered_free = sem("gathered_free")
        fill_begun = sem("fill_begun")
        rows_in = [sem(f"rows_in{s}") for s in range(SLOTS)]
        added = sem("added")
        gathered_ready = sem("gathered_ready")
        gathered_stored = sem("gathered_stored")

        def group(f, h, c, i):
            return f * (2 * GROUPS) + c * PER_CHUNK + (h * GROUPS + i + 1)

        def buffer_p(i):
            return (0, 0) if i < 0 else (1 + i // 2, i % 2)

        def pair(h, i):
            return pairs[(h + i + 1) % SETS]

        def tile(b, k):
            return FIRST[k] + b if UP[k] else FIRST[k] + TAKES[k] - 1 - b

        def first_in_buffer(k):
            return BUFFER.index(BUFFER[k]) == k

        def known(n, below):
            return isinstance(n, int) and n < below

        block = ctx.enter_context(nc.Block())

        @block.sync
        def _(sp):
            sp.dma_start(look_id[:, FIRST_COLUMNS], lookup_ids[:, FIRST_COLUMNS]).then_inc(first_lookups_in, 16)
            sp.dma_start(look_len[:, FIRST_COLUMNS], lookup_lengths[:, FIRST_COLUMNS]).then_inc(first_lookups_in, 16)
            sp.dma_start(place[:], lookup_place).then_inc(ramps_in, 16)
            sp.dma_start(ramp[:], ramps).then_inc(ramps_in, 16)
            sp.dma_start(look_id[:, OTHER_COLUMNS], lookup_ids[:, OTHER_COLUMNS]).then_inc(other_lookups_in, 16)
            sp.dma_start(look_len[:, OTHER_COLUMNS], lookup_lengths[:, OTHER_COLUMNS]).then_inc(other_lookups_in, 16)
            sp.sem_inc(pooled_free, 1)

            def load(f, c):
                src = table_rows[bass.ds(f * V, J * P), :].rearrange("(p j) e -> p (j e)", j=J)
                sp.dma_start(table[:, 0, c * CE:(c + 1) * CE], src[:, c * CE:(c + 1) * CE]).then_inc(table_in[c], 16)

            def report(f, c):
                sp.wait_ge(table_in[c], f * 16 + 16)
                sp.sem_inc(table_landed, 1)

            def store(f):
                sp.wait_ge(pooled_ready, f + 1)
                sp.dma_start(counted_rows[:, :, bass.ds(f * E, E)],
                             pooled[:].rearrange("p (m e) -> p m e", e=E)).then_inc(pooled_stored, 16)

            def free_pooled(f):
                sp.wait_ge(pooled_stored, f * 16 + 16)
                sp.sem_inc(pooled_free, 1)

            for c in range(CHUNKS):
                load(0, c)
            for c in range(CHUNKS):
                report(0, c)
            def feature(f):
                for c in range(CHUNKS):
                    if c < CHUNKS - 1:
                        sp.wait_ge(table_used, (f - 1) * (CHUNKS - 1) + (c + 1))
                    else:
                        sp.wait_ge(sums_done, 2 * f)
                    load(f, c)
                    if c:
                        report(f, c - 1)
                    if not known(f, 2):
                        if c == 1:
                            store(f - 2)
                        if c == 2:
                            free_pooled(f - 2)
                report(f, CHUNKS - 1)

            feature(1)
            with sp.Fori(2, M) as f:
                feature(f)
            for f in range(M - 2, M):
                store(f)
                free_pooled(f)

        @block.gpsimd
        def _(pool):
            for out, pattern, base, by in (
                (value, [[1, L + 1]], 0, 0),
                (first_row, [[V, G], [0, L]], M * V, 0),
                (position, [[0, G], [1, L]], 0, 0),
                (records[:, :, L], [[P, TILES]], 0, 1),
            ) + tuple(
                (last_rank[:, COLUMN[k]:COLUMN[k] + TAKES[k]], [[P if UP[k] else -P, TAKES[k]]], tile(0, k) * P + P - 1, 0)
                for k in range(SLOTS)
            ):
                nc.gpsimd.iota(out, pattern=pattern, base=base, channel_multiplier=by).then_inc(iotas_done, 1)
            last_row = pool.to_reg(F * V - 1)
            pool.sem_inc(gathered_free, 1)
            room = BUFFERS * L * E - TILES * RECORD
            all_rows = rows[:].rearrange("p s n -> p (s n)")
            nc.gpsimd.memset(all_rows[:, 0:room], 0.0).then_inc(rows_zeroed, 1)
            pool.wait_ge(records_ready, 1)
            for t in range(TILES):
                nc.gpsimd.indirect_dma_start(
                    out=sorted_records, out_offset=bass.IndirectOffsetOnAxis(ap=rank[:, t:t + 1], axis=0),
                    in_=records[:, t, :], in_offset=None).then_inc(records_out, 16)
            pool.wait_ge(records_out, 16 * TILES)
            for k in range(SLOTS):
                if first_in_buffer(k):
                    nc.gpsimd.dma_start(row_now[:, BUFFER[k], :],
                                        sorted_records[tile(0, k) * P:(tile(0, k) + 1) * P, :]).then_inc(first_rows_in, 16)
            nc.gpsimd.memset(record_words, 0).then_inc(records_gone, 1)
            pool.wait_ge(records_gone, 1)
            pool.wait_ge(rows_zeroed, 1)
            for k in range(SLOTS):
                if first_in_buffer(k):
                    pool.sem_inc(buffer_zeroed[k], 1)
            pool.wait_ge(depths_ready, 1)
            pool.wait_ge(first_rows_in, 16 * BUFFERS)

            def gather(b, k):
                pool.wait_ge(buffer_zeroed[k], b + 1)
                refills = b if first_in_buffer(k) else b + 1
                if not known(refills, 1):
                    pool.wait_ge(row_now_in[k], refills * 16)
                pool.sem_inc(fill_begun, 1)
                n = pool.value_load(depth[0:1, bass.ds(b + COLUMN[k], 1)], min_val=1, max_val=L)
                with ExitStack() as deeper:
                    for l in range(L):
                        if l:
                            deeper.enter_context(pool.If(n > l))
                        nc.gpsimd.indirect_dma_start(
                            out=rows[:, BUFFER[k], l * E:(l + 1) * E], out_offset=None, in_=table_rows,
                            in_offset=bass.IndirectOffsetOnAxis(ap=row_now[:, BUFFER[k], l:l + 1], axis=0),
                            bounds_check=last_row, oob_is_err=False).then_inc(rows_in[k], 16)

            def put(b, slots):
                pool.wait_ge(gathered_ready, b + 1)
                pool.sem_inc(fill_begun, 1)
                for k in range(slots):
                    nc.gpsimd.indirect_dma_start(
                        out=out_gathered, out_offset=bass.IndirectOffsetOnAxis(ap=place_now[:, k:k + 1], axis=0),
                        in_=gathered[:, k * E:(k + 1) * E], in_offset=None).then_inc(gathered_stored, 16)

            def free_gathered(b):
                pool.wait_ge(gathered_stored, (b + 1) * (16 * SLOTS))
                pool.sem_inc(gathered_free, 1)

            def batch(b, slots, first=False):
                for k in range(slots):
                    if k == 2 and not first:
                        put(b - 1, SLOTS)
                    if k == 4 and not first:
                        free_gathered(b - 1)
                    gather(b, k)
                if not first and slots < 3:
                    put(b - 1, SLOTS)
                if not first and slots < SLOTS:
                    free_gathered(b - 1)

            batch(0, SLOTS, first=True)
            with pool.Fori(1, FULL) as b:
                batch(b, SLOTS)
            batch(FULL, EXTRA)
            put(FULL, EXTRA)
            pool.wait_ge(gathered_stored, 16 * TILES)

        @block.scalar
        def _(act):
            act.dma_start(len_tile.rearrange("p (k f) -> p k f", k=BLOCKS),
                          lengths[:, M:F].rearrange("(k p) f -> p k f", p=P)).then_inc(lengths_in, 16)
            act.dma_start(tri, triangle).then_inc(lengths_in, 16)
            act.dma_start(id_tile, ids[:, M:F, :].rearrange("(k p) f l -> p k (f l)", p=P)).then_inc(gather_ids_in, 16)

            def save_counts(f, h, c, i):
                g = PER_CHUNK * c + (i + 1)
                act.wait_ge(counted, group(f, h, c, i) + 1)
                dst = counts[h][:, :, bass.ds(g * GROUP, GROUP)].rearrange("p j (t b) -> p t j b", t=2)
                src = pair(h, i)[:, :, 0:WIDE].rearrange("p t (j b) -> p t j b", b=TRIO)
                nc.scalar.activation(dst, src, ACT.Copy).then_inc(counts_saved, 1)

            def refill(b, k):
                act.wait_ge(added, b * SLOTS + (k + 1))
                n, later = NEXT[k]
                act.dma_start(row_now[:, BUFFER[k], :],
                              sorted_records[bass.ds(tile(b + later, n) * P, P), :]).then_inc(row_now_in[n], 16)
                nc.scalar.activation(rows[:, BUFFER[k], :], zero[:].to_broadcast([P, L * E]),
                                     ACT.Copy).then_inc(buffer_zeroed[n], 1)

            def feature(f):
                for h in range(2):
                    save_counts(f, h, 0, -1)
                    turns = (((0, 4, 2, (1,)), (4, 6, 2, (2,)), (6, CHUNKS, 2, ())),
                             ((0, 1, 2, (3,)), (1, 6, 2, (4,)), (6, CHUNKS, 1, (0,))))[h]
                    if h == 1 and isinstance(f, int) and f == 1:
                        turns = (0, BEGIN + 1, 1, (0,)), (BEGIN + 1, CHUNKS, 1, ())
                    for lo, hi, back, slots in turns:
                        with act.Fori(lo, hi) as c:
                            for i in range(PER_CHUNK):
                                save_counts(f, h, c, i)
                        for k in slots:
                            if not isinstance(f, int) or refilled(f - back, k):
                                refill(f - back, k)

            def refilled(b, k):
                n, later = NEXT[k]
                return 0 <= b < TAKES[k] and b + later < TAKES[n]

            for f in range(2):
                feature(f)
            with act.Fori(2, FULL) as f:
                feature(f)
            for f in range(FULL, M):
                feature(f)
            for b in range(M - 2, FULL + 1):
                for k in range(SLOTS):
                    if (b > M - 2 or k > 0) and refilled(b, k):
                        refill(b, k)

        @block.tensor
        def _(pe):
            def count(f, h, c, i):
                n = group(f, h, c, i)
                pe.wait_ge(onehots_ready, n + 1)
                free = n - (SETS - 2 if h == 0 and c == 0 and i < 1 else SETS - 1)
                if not known(free, 1):
                    pe.wait_ge(counts_saved, free)
                k, x = buffer_p(i)
                for t in range(2):
                    last = nc.tensor.matmul(pair(h, i)[:, t, 0:WIDE], onehot_p[64 * t:64 * t + 64, k, :, x],
                                            onehot_j[64 * t:64 * t + 64, i + 1, :], start=True, stop=True)
                last.then_inc(counted, 1)

            parts = table[:].bitcast(BF16).rearrange("p t (j e x) -> p t j e x", e=E, x=2)

            def multiply(h, j0, j1):
                for j in range(j0, j1):
                    for k in range(HALF // P):
                        last = nc.tensor.matmul(sums[h][:, k * PARTS * E:(k + 1) * PARTS * E],
                                                counts[h][:, j, k * P:(k + 1) * P], parts[:, :, j, :, 1],
                                                start=(j == 0 and k == 0), stop=(j == J - 1), skip_group_check=True)
                if j1 == J:
                    last.then_inc(sums_done, 1)
                elif h == 1 and j1 % JC == 0:
                    last.then_inc(table_used, 1)

            def phase(f, h, with_counts=True, with_products=True):
                if with_counts:
                    count(f, h, 0, -1)
                if with_products:
                    pe.wait_ge(counts_saved, group(f, h, 0, -1))
                    free = 2 * f + (h - 1)
                    if not known(free, 1):
                        pe.wait_ge(sums_read, free)
                for c in range(CHUNKS):
                    for i in range(PER_CHUNK):
                        if with_counts:
                            count(f, h, c, i)
                        if with_products:
                            if h == 1 and i == 0:
                                pe.wait_ge(parts_ready, f * CHUNKS + (c + 1))
                            multiply(1 - h, c * JC + i * JC // PER_CHUNK, c * JC + (i + 1) * JC // PER_CHUNK)
                    if c == 0 and not with_products:
                        rank_lengths()

            def rank_lengths():
                pe.wait_ge(length_counts, 1)
                nc.tensor.matmul(sums[0][:, 0:L + 1], tri[:, 0:P], has_sum, start=True, stop=False)
                nc.tensor.matmul(sums[0][:, 0:L + 1], tri[:, P:2 * P], before_h, start=False, stop=True)
                nc.tensor.matmul(sums[1][:, 0:L + 1], tri[:, P:2 * P], before_h, start=True, stop=True).then_inc(ranked, 1)

            phase(0, 0, with_products=False)
            phase(0, 1)
            with pe.Fori(1, M) as f:
                for h in range(2):
                    phase(f, h)
            phase(M, 0, with_counts=False)

        @block.vector
        def _(dve):
            done = [0]

            def step(ins):
                done[0] += 1
                ins.then_inc(prepared, 1)
                dve.wait_ge(prepared, done[0])

            def rows_of_block(k):
                idx = records[:, k * G:(k + 1) * G, 0:L]
                lens = len_tile[:, k * G:(k + 1) * G].unsqueeze(2).to_broadcast([P, G, L])
                nc.vector.tensor_tensor(masked, position, lens, ALU.is_ge)
                step(nc.vector.tensor_tensor(idx, id_tile[:, k, :].rearrange("p (f l) -> p f l", l=L), first_row, ALU.add))
                step(nc.vector.scalar_tensor_tensor(out=idx, in0=masked, scalar=float(SKIP), in1=idx,
                                                    op0=ALU.mult, op1=ALU.add))

            def by_value(x):
                return x.rearrange("p (v t) -> p v t", t=TILES)

            def over_tiles(x):
                return x.unsqueeze(2).to_broadcast([P, L + 1, TILES])

            def count_lengths():
                step(nc.vector.tensor_scalar(length, len_tile, 0.0, float(L), ALU.max, ALU.min))
                step(nc.vector.tensor_tensor(by_value(has), length.unsqueeze(1).to_broadcast([P, L + 1, TILES]),
                                             over_tiles(value), ALU.is_equal))
                step(nc.vector.tensor_tensor_scan(until, has, has, 0.0, ALU.add, ALU.max))
                ends = by_value(until)[:, :, TILES - 1]
                nc.vector.memset(before[:, 0:1], 0.0)
                step(nc.vector.tensor_copy(before[:, 1:L + 1], ends[:, 0:L]))
                nc.vector.tensor_copy(before_h, before)
                nc.vector.tensor_tensor(has_sum, ends, before, ALU.subtract).then_inc(length_counts, 1)

            def rank_bags():
                dve.wait_ge(ranked, 1)
                step(nc.vector.scalar_tensor_tensor(out=shift, in0=sums[0][:, 0:L + 1], scalar=-1.0, in1=before,
                                                    op0=ALU.add, op1=ALU.subtract))
                nc.vector.tensor_copy(below, sums[1][:, 0:L + 1])
                step(nc.vector.tensor_tensor(by_value(until), by_value(until), over_tiles(shift), ALU.add))
                step(nc.vector.tensor_tensor(until, until, has, ALU.mult))
                step(nc.vector.tensor_reduce(out=rank_f, in_=until.rearrange("p (v t) -> p t v", t=TILES),
                                             axis=AX_X, op=ALU.add))
                nc.vector.tensor_copy(rank, rank_f).then_inc(records_ready, 1)

            def find_depths():
                fits = has[:, 0:TILES * L].rearrange("p (t l) -> p t l", l=L)
                step(nc.vector.tensor_tensor(fits, below[:, 1:L + 1].unsqueeze(1).to_broadcast([P, TILES, L]),
                                             last_rank.unsqueeze(2).to_broadcast([P, TILES, L]), ALU.is_le))
                step(nc.vector.tensor_reduce(out=depth_f, in_=fits, axis=AX_X, op=ALU.add))
                step(nc.vector.tensor_scalar(depth_f, depth_f, 1.0, None, ALU.max))
                for k in range(SLOTS):
                    mine = slice(COLUMN[k], COLUMN[k] + TAKES[k])
                    nc.vector.tensor_tensor_scan(arrival_f[:, mine], depth_f[:, mine], depth_f[:, mine], 0.0, ALU.add, ALU.max)
                step(nc.vector.tensor_copy(depth[:], depth_f))
                step(nc.vector.tensor_scalar(arrival[:], arrival_f, 16.0, None, ALU.mult))
                dve.sem_inc(depths_ready, 1)

            def columns_of_lookups(part):
                a, b = work_a[:, part], work_b[:, part]
                step(nc.vector.tensor_scalar(a, look_id[:, part], 1.0 / J, 0.5 / J - 0.5, ALU.mult, ALU.add))
                step(nc.vector.tensor_scalar(b, a, MAGIC, MAGIC, ALU.add, ALU.subtract))
                nc.vector.tensor_copy(p_of[:, part], b)
                step(nc.vector.scalar_tensor_tensor(out=a, in0=b, scalar=-float(J), in1=look_id[:, part],
                                                    op0=ALU.mult, op1=ALU.add))
                step(nc.vector.tensor_scalar(b, a, float(TRIO), place[:, 1:2], ALU.mult, ALU.add))
                step(nc.vector.scalar_tensor_tensor(out=j_of[:, part], in0=look_len[:, part], scalar=place[:, 0:1], in1=b,
                                                    op0=ALU.is_gt, op1=ALU.mult))

            def between(c):
                if c == 0:
                    dve.wait_ge(iotas_done, 4 + SLOTS)
                    dve.wait_ge(lengths_in, 32)
                    count_lengths()
                elif c <= 2:
                    if c == 1:
                        dve.wait_ge(gather_ids_in, 16)
                    for k in range((c - 1) * BLOCKS // 2, c * BLOCKS // 2):
                        rows_of_block(k)
                elif c == 3:
                    rank_bags()
                elif c == 5:
                    dve.wait_ge(other_lookups_in, 32)
                    columns_of_lookups(OTHER_COLUMNS)
                elif c == 6:
                    find_depths()

            ramp_twice = ramp[:, 0:2 * P].rearrange("p (n x) -> p n x", x=2)

            def onehots(f, h, c, i):
                n = group(f, h, c, i)
                free = n - (PER_CHUNK - 2) if i % 2 == 0 else n - (PER_CHUNK - 1)
                if not known(free, 1):
                    dve.wait_ge(counted, free)
                k, x = buffer_p(i)
                if i < 0:
                    nc.vector.tensor_scalar(onehot_p[:, k, :, x], ramp_twice[:, :, 0], p_of[:, bass.ds(n, 1)], None,
                                            ALU.is_equal)
                elif x == 0:
                    mine = p_now[:, h, bass.ds(c * PER_CHUNK + (i + 1), 2)]
                    nc.vector.tensor_tensor(onehot_p[:, k, :, :], ramp_twice,
                                            mine.unsqueeze(1).to_broadcast([P, P, 2]), ALU.is_equal)
                nc.vector.tensor_scalar(onehot_j[:, i + 1, :], ramp[:, 2 * P:], j_of[:, bass.ds(n, 1)], None,
                                        ALU.is_equal).then_inc(onehots_ready, 1)

            def start_half(f, h):
                nc.vector.tensor_copy(p_now[:, h, :], p_of[:, bass.ds(group(f, h, 0, -1), GROUPS)]).then_inc(p_now_ready, 1)
                onehots(f, h, 0, -1)
                dve.wait_ge(p_now_ready, 2 * f + (h + 1))
                dve.sem_inc(waited, 1)

            def upper_halves(t):
                return table[:, t, :].bitcast(BF16).rearrange("p (n x) -> p n x", x=2)[:, :, 1]

            def cut_rest(f, c, part, parts, k):
                sl = bass.ds(c * CE + part * CE // parts, CE // parts)
                if part == 0:
                    dve.wait_ge(table_landed, f * CHUNKS + c + 1)
                nc.vector.tensor_tensor(table[:, 1, sl], table[:, 0, sl], upper_halves(0)[:, sl],
                                        ALU.subtract).then_inc(rest_done, 1)

            def cut_low(f, c, part, parts, k):
                sl = bass.ds(c * CE + part * CE // parts, CE // parts)
                dve.wait_ge(rest_done, f * (CHUNKS + SLOW) + k + 1)
                cut = nc.vector.tensor_tensor(table[:, 2, sl], table[:, 1, sl], upper_halves(1)[:, sl], ALU.subtract)
                if part == parts - 1:
                    cut.then_inc(parts_ready, 1)

            def nan_to_num(y, x, k):
                w = x.shape[1]
                nc.vector.tensor_tensor(is_nan[:, 0:w], x, x, ALU.not_equal).then_inc(clean_step, 1)
                nc.vector.tensor_scalar(y, x, FMAX, -FMAX, ALU.min, ALU.max).then_inc(clean_step, 1)
                dve.wait_ge(clean_step, k * 2 + 2)
                dve.sem_inc(waited, 1)
                return nc.vector.copy_predicated(y, is_nan[:, 0:w], zero[:].to_broadcast([P, w]))

            def read_sums(f, h):
                dve.wait_ge(sums_done, 2 * f + (h + 1))
                if h == 0:
                    dve.wait_ge(pooled_free, f + 1)
                nc.vector.tensor_reduce(
                    out=pooled[:, 2 * h * E:2 * (h + 1) * E].rearrange("p (k e) -> p k e", e=E),
                    in_=sums[h][:, 0:2 * PARTS * E].rearrange("p (k t e) -> p k e t", t=PARTS, e=E),
                    axis=AX_X, op=ALU.add).then_inc(sums_read, 1)

            def clean_pooled(f, uses):
                dve.wait_ge(sums_read, 2 * f + 3)
                nan_to_num(pooled[:], pooled[:], uses).then_inc(pooled_ready, 1)

            def add_rows(b, k):
                rows_then = dve.value_load(arrival[0:1, bass.ds(b + COLUMN[k], 1)], min_val=16, max_val=16 * L * (FULL + 1))
                dve.wait_ge(rows_in[k], rows_then)
                nc.vector.tensor_reduce(out=summed[:, k * E:(k + 1) * E],
                                        in_=rows[:, BUFFER[k], :].rearrange("p (l e) -> p e l", e=E),
                                        axis=AX_X, op=ALU.add)
                nc.vector.tensor_copy(place_summed[:, k:k + 1], row_now[:, BUFFER[k], L:L + 1]).then_inc(added, 1)

            def clean_gathered(b, slots, uses):
                dve.wait_ge(added, b * SLOTS + slots)
                dve.wait_ge(gathered_free, b + 1)
                nc.vector.tensor_copy(place_now[:, 0:slots], place_summed[:, 0:slots])
                nan_to_num(gathered[:, 0:slots * E], summed[:, 0:slots * E], uses).then_inc(gathered_ready, 1)

            def chunk(f, h, c, *cut):
                for i in range(PER_CHUNK):
                    onehots(f, h, c, i)
                    if cut and i == 1:
                        cut_rest(f, *cut)
                    if cut and i == 4:
                        cut_low(f, *cut)

            def feature(f):
                served = not known(f, 2)
                start_half(f, 0)
                with dve.Fori(0, LAG - 1) as c:
                    chunk(f, 0, c)
                if served:
                    clean_pooled(f - 2, uses_before(f))
                chunk(f, 0, LAG - 1)
                if served:
                    add_rows(f - 2, 1)
                for c in range(SLOW):
                    chunk(f, 0, c * 2 + LAG, c, 0, 2, c * 2)
                    chunk(f, 0, c * 2 + (LAG + 1), c, 1, 2, c * 2 + 1)
                    if c == 0:
                        read_sums(f - 1, 0)
                    if served:
                        add_rows(f - 2, c + 2)
                second_half(f)

            def second_half(f):
                served = not known(f, 2)
                start_half(f, 1)
                very_first = isinstance(f, int) and f == 1
                for lo, hi in ((0, BEGIN), (BEGIN, CHUNKS - SLOW)) if very_first else ((0, CHUNKS - SLOW),):
                    with dve.Fori(lo, hi) as c:
                        chunk(f, 1, c, c + SLOW, 0, 1, c + 2 * SLOW)
                    if very_first and hi == BEGIN:
                        add_rows(0, 0)
                if served:
                    add_rows(f - 2, 4)
                if not known(f, 1):
                    read_sums(f - 1, 1)
                chunk(f, 1, CHUNKS - 2)
                if served:
                    clean_gathered(f - 2, SLOTS, uses_before(f) + 1)
                if served:
                    add_rows(f - 1, 0)
                chunk(f, 1, CHUNKS - 1)

            def uses_before(f):
                return 2 * f - 4

            def first_half_of_all():
                start_half(0, 0)
                for c in range(CHUNKS):
                    if c < LAG:
                        chunk(0, 0, c)
                    else:
                        k = c - LAG
                        chunk(0, 0, c, k // 2, k % 2, 2, k)
                    between(c)

            nc.vector.memset(zero[:], 0.0)
            dve.sem_inc(sums_read, 1)
            dve.wait_ge(ramps_in, 32)
            dve.wait_ge(first_lookups_in, 32)
            columns_of_lookups(FIRST_COLUMNS)

            first_half_of_all()
            second_half(0)
            feature(1)
            with dve.Fori(2, M) as f:
                feature(f)
            dve.wait_ge(gathered_ready, M - 2)
            clean_pooled(M - 2, uses_before(M))
            uses = uses_before(M) + 1
            for b in range(M - 2, FULL + 1):
                slots = SLOTS if b < FULL else EXTRA
                for k in range(EARLY if b == M - 2 else 0, slots):
                    add_rows(b, k)
                clean_gathered(b, slots, uses)
                uses += 1
            for h in range(2):
                read_sums(M - 1, h)
            clean_pooled(M - 1, uses)


def kernel(r_ids, r_lengths, L0_rec_tables):
    import numpy as np
    import concourse.bacc as bacc
    from concourse.bass_utils import run_bass_kernel_spmd

    ids, lengths, tables = (np.ascontiguousarray(a) for a in (r_ids, r_lengths, L0_rec_tables))
    B, F, L = ids.shape
    _, V, E = tables.shape
    J, HALF, GROUPS = geometry(B, V)
    TILES = B // P * (F - M)

    def by_group(a):
        padded = np.zeros((2, GROUPS * GROUP, M, L), a.dtype)
        padded[:, :HALF] = a.reshape(2, HALF, M, L)
        there = np.zeros((2, 64, M, 2, GROUPS), a.dtype)
        there[:, :TRIO * L] = padded.reshape(2, GROUPS, 2, TRIO, M, L).transpose(2, 3, 5, 4, 0, 1).reshape(
            2, TRIO * L, M, 2, GROUPS)
        return there.reshape(P, M * 2 * GROUPS)

    place = np.zeros((2, 64, 2), np.float32)
    place[:, :, 0] = 1 << 20
    place[:, :TRIO * L, 0] = np.arange(TRIO * L) % L
    place[:, :TRIO * L, 1] = 1 + np.arange(TRIO * L) // L
    ramps = np.concatenate([np.arange(2 * P) // 2, 1 + np.arange(J * TRIO)]).astype(np.float16)
    arrays = {
        "ids": ids,
        "lengths": lengths,
        "tables": tables,
        "lookup_ids": by_group(ids[:, :M]),
        "lookup_lengths": by_group(np.broadcast_to(lengths[:, :M, None], (B, M, L))),
        "lookup_place": place.reshape(P, 2),
        "ramps": np.tile(ramps, (P, 1)),
        "triangle": np.concatenate([np.triu(np.ones((P, P)), 1), np.ones((P, P))], axis=1).astype(np.float16),
    }
    nc = bacc.Bacc("TRN2", target_bir_lowering=False, num_devices=1, dynamic_dma_scratch_size=DMA_SCRATCH)
    args = [nc.dram_tensor(n, a.shape, mybir.dt.from_np(a.dtype), kind="ExternalInput").ap()
            for n, a in arrays.items()]
    args.append(nc.dram_tensor("out_counted", (B, M * E), F32, kind="ExternalOutput").ap())
    args.append(nc.dram_tensor("out_gathered", (TILES * P, E), F32, kind="ExternalOutput").ap())
    build_embedding_bag(nc, *args)
    got = run_bass_kernel_spmd(nc, [arrays], core_ids=[0]).results[0]
    tiles = got["out_gathered"].reshape(B // P, F - M, P, E).transpose(0, 2, 1, 3).reshape(B, (F - M) * E)
    return np.concatenate([got["out_counted"], tiles], axis=1)
```
